# Optimizing a Trainium2 kernel written in Bass

```python
import numpy as np
import jax
import jax.numpy as jnp

def _softmax(x, axis=-1):
    return jax.nn.softmax(x, axis=axis)
def _gelu(x):
    return jax.nn.gelu(x, approximate=True)
def _silu(x):
    return jax.nn.silu(x)
def _sigmoid(x):
    return jax.nn.sigmoid(x)
def _layernorm(x, axis=-1, eps=1e-5):
    m = jnp.mean(x, axis=axis, keepdims=True)
    v = jnp.var(x, axis=axis, keepdims=True)
    return (x - m) / jnp.sqrt(v + eps)
def _scatter_add(tgt, idx, src, axis=0):
    return tgt.at[idx].add(src)
def _segment_sum(src, seg, n):
    return jax.ops.segment_sum(src, seg, n)

kernel_name = 'mk_adj_resnorm_d1_adj_256_247aac'

def setup_inputs(seed: int = 0):
    np.random.seed(seed)
    _w = jnp.asarray
    def _rec_inputs():
        import jax
        import jax.numpy as jnp
        _gk = jax.random.key(seed)
        x = -0.0005207 + 1.001 * jax.random.normal(jax.random.fold_in(_gk, 1), (8192, 256), jnp.float32)
        _w = (1.0 + jnp.arange(8192, dtype=jnp.float32)) ** -0.5
        _w = _w / _w.mean()
        _pij = jnp.clip(0.00390625 * _w[:, None] * _w[None, :], 0.0, 1.0)
        _a = jax.random.uniform(jax.random.fold_in(_gk, 2), (8192, 8192)) < _pij
        _af = _a.astype(jnp.float32)
        adj = _af
        return x, adj
    x, adj = _rec_inputs()
    def _L0_gnn_setup():
        import jax, jax.numpy as jnp
        import numpy as np
        N = 8192
        IN_DIM = 512
        HID = 256
        REL_DIM = 256
        key = jax.random.key(seed)
        ks = jax.random.split(key, 8)
        s = 1.0 / np.sqrt(IN_DIM)
        return {'relation': jax.random.normal(ks[0], (N, REL_DIM), dtype=jnp.float32), 'context': jax.random.normal(ks[1], (N, IN_DIM), dtype=jnp.float32), 'adj_tensor': jax.random.randint(ks[2], (N, N), 0, 2).astype(jnp.float32), 'W_common': jax.random.normal(ks[3], (HID, IN_DIM), dtype=jnp.float32) * s, 'w_left': jax.random.normal(ks[4], (HID,), dtype=jnp.float32) * (1.0 / np.sqrt(HID)), 'b_left': jax.random.normal(ks[5], (), dtype=jnp.float32) * 0.01, 'w_right': jax.random.normal(ks[6], (HID,), dtype=jnp.float32) * (1.0 / np.sqrt(HID)), 'b_right': jax.random.normal(ks[7], (), dtype=jnp.float32) * 0.01}
    _L0_gnn_all = _L0_gnn_setup()
    _L0_gnn_in = {k: v for k, v in _L0_gnn_all.items() if k in ('context', 'W_common', 'w_left', 'b_left', 'w_right', 'b_right', )}
    del _L0_gnn_all

    return {
        "x": x,
        "adj": adj,
        "L0_gnn_context": _L0_gnn_in["context"],
        "L0_gnn_W_common": _L0_gnn_in["W_common"],
        "L0_gnn_w_left": _L0_gnn_in["w_left"],
        "L0_gnn_b_left": _L0_gnn_in["b_left"],
        "L0_gnn_w_right": _L0_gnn_in["w_right"],
        "L0_gnn_b_right": _L0_gnn_in["b_right"],
    }

def reference(x, adj, L0_gnn_context, L0_gnn_W_common, L0_gnn_w_left, L0_gnn_b_left, L0_gnn_w_right, L0_gnn_b_right):
    import jax
    import jax.numpy as jnp
    def _L0_gnn_ref(relation, context, adj_tensor, W_common, w_left, b_left, w_right, b_right):
        import jax, jax.numpy as jnp
        import numpy as np
        N = 8192
        IN_DIM = 512
        HID = 256
        REL_DIM = 256
        in_fts = context @ W_common.T
        left = in_fts @ w_left + b_left
        right = in_fts @ w_right + b_right
        logits = left[:, None] + right[None, :]
        logits = jnp.where(logits >= 0, logits, 0.2 * logits)
        logits = jnp.where(adj_tensor <= 0.0, -jnp.inf, logits)
        coefs = jax.nn.softmax(logits, axis=-1)
        x = coefs @ relation
        return jax.nn.relu(x)

    x = _layernorm(x + _L0_gnn_ref(x, L0_gnn_context, adj, L0_gnn_W_common, L0_gnn_w_left, L0_gnn_b_left, L0_gnn_w_right, L0_gnn_b_right), axis=-1)
    return x


_drawn_inputs = setup_inputs


def setup_inputs(seed=0):
    import zlib

    import numpy as np

    out = dict(_drawn_inputs(seed))
    spreads = {}
    factors = {}
    for name, (base, spread) in spreads.items():
        noise = np.random.default_rng([zlib.crc32(name.encode()), seed]).standard_normal(out[name].shape)
        drawn = base * np.exp(spread * noise) if base else spread * noise
        out[name] = jnp.asarray(drawn.astype(out[name].dtype))
    for name, factor in factors.items():
        out[name] = (out[name] * factor).astype(out[name].dtype)
    return out
```

```python
import concourse.bass as bass
from concourse import mybir
from contextlib import ExitStack

F32 = mybir.dt.float32
F16 = mybir.dt.float16
I32 = mybir.dt.int32
ALU = mybir.AluOpType
ACT = mybir.ActivationFunctionType
AX = mybir.AxisListType
RMAX = bass.bass_isa.ReduceOp.max


def build(nc, x, adj, ctx_in, w_common, w_left, b_left, w_right, b_right, out):
    N, D = x.shape
    CIN = ctx_in.shape[1]
    HID = w_common.shape[0]
    P = 128
    Q = 4
    B = P // Q
    NQ = N // Q
    JB = NQ // B
    NS = N // B
    SG = P // B
    NG = N // P
    JS = 40
    CS = JS * B
    XW = D + 2
    NB = 4
    GI = 2
    SI = GI * SG
    IT = NG // GI
    CT = 8
    NCH = N // P // CT
    XC = 8
    BIG = 2.0 ** 100
    PSCALE = 2.0 ** 15
    SPREAD = 10.0
    SLOPE = 0.2
    EPS = 1e-5
    FLOOR = -1e28
    GEN = 15
    FSCALE = 2.0 ** 14

    stack = ExitStack()
    with stack:
        def sb(name, shape, dt=F32):
            return stack.enter_context(nc.sbuf_tensor(name, shape, dt))

        def sem(name):
            return stack.enter_context(nc.semaphore(name))

        X = sb("X", [P, JB, XW])
        T = sb("T", [P, 2, JB, P])
        strip = sb("strip", [P, NB, NQ])
        pair = sb("pair", [P, 2, CS])
        w = sb("w", [P, 2, NQ])
        tab = sb("tab", [P, NQ])
        lb = sb("lb", [P, NS])
        b1 = sb("b1", [P, NS])
        b2 = sb("b2", [P, NS])
        xrow = sb("xrow", [P, 2, D])
        y = sb("y", [P, 2, D + 1])
        ident = sb("ident", [P, P])
        small = sb("small", [P, 64])
        const = sb("const", [P, 4])
        LR = sb("LR", [P, 2, JB])
        lrep = sb("lrep", [P, 2, Q, B])
        rcol = sb("rcol", [JB, Q, B])
        F = sb("F", [P, JB])
        Fx = sb("Fx", [P, JB])
        wcol = sb("wcol", [P, 2, HID // P])
        bias = sb("bias", [P, 2])
        W = strip[:, 3, 0:2 * CIN].rearrange("p (h k) -> p h k", h=2)
        wrep = strip[:, 3, 2 * CIN:2 * CIN + 4 * P].rearrange("p (c h m) -> p c h m", c=2, h=2)
        vb = w[:, 0, 0:2 * CIN].rearrange("p (c k) -> p c k", c=2)
        xs = T[:, :, :, :].rearrange("p b j m -> p (b j m)").rearrange("p (j d) -> p j d", d=D)
        Xflat = X[:, :, :].rearrange("p j w -> p (j w)")
        X16 = Xflat.bitcast(F16).rearrange("p (j w) -> p j w", w=2 * XW)
        T16 = T[:, :, :, :].rearrange("p b j m -> p (b j m)").bitcast(F16).rearrange(
            "p (b j m e) -> p b j m e", b=2, j=JB, e=2)
        pair16 = pair[:, :, :].rearrange("p b c -> p (b c)").bitcast(F16).rearrange(
            "p (b c e) -> p b c e", b=2, e=2)
        cstage = [Xflat[:, s * CT * CIN:(s + 1) * CT * CIN].rearrange("p (t k) -> p t k", k=CIN) for s in range(4)]

        mx3, amx = small[:, 0:3], small[:, 4:7]
        pe2, inv, sc = small[:, 8:9], small[:, 9:10], small[:, 10:11]
        spread = small[:, 11:12]
        flag = small[:, 12:13]
        flagf, fast, tscale = small[:, 13:14], small[:, 14:15], small[:, 15:16]
        neg_spread = small[:, 24:25]
        mnq, m1, mn = small[:, 16:17], small[:, 17:18], small[:, 18:19]
        c4 = small[:, 20:24]
        nmax = small[:, 19:20]

        def st(name_col, o):
            return small[:, 28 + 14 * o + name_col:29 + 14 * o + name_col]

        ps = [stack.enter_context(nc.psum_tensor(f"ps{i}", [P, 512], F32)) for i in range(2)]
        pt = stack.enter_context(nc.psum_tensor("pt", [P, 512], F32))
        lr_dram = nc.dram_tensor("lr_scratch", [2, N], F32, kind="Internal").ap()

        s_const = sem("constants_ready")
        s_half = sem("half_variance_ready")
        s_w = sem("weights_in")
        s_ctx = [sem(f"context_in{s}") for s in range(4)]
        s_x = sem("x_in")
        s_wrep = sem("w_replicated")
        s_v = sem("v_ready")
        s_psfree = sem("psum_evacuated")
        s_prod = sem("product_ready")
        s_sum = sem("product_summed")
        s_dot = sem("right_dots_done")
        s_lr = sem("left_right_ready")
        s_lrout = sem("left_right_stored")
        s_tab = sem("tables_in")
        s_mx = sem("partial_maxima")
        s_amx = sem("overall_maxima")
        s_id = sem("identity_ready")
        s_rep = sem("left_replicated")
        s_lT = sem("left_transposed")
        s_sc = sem("x_scale_ready")
        s_xh = sem("x_high_ready")
        s_tabs = sem("bias_tables_ready")
        s_xrdy = sem("x_low_and_ones_ready")
        s_setup = sem("vector_setup_steps")
        s_adj = [sem(f"adj_in{b}") for b in range(NB)]
        s_rT = sem("right_transposed")
        s_F = sem("factor_steps")
        s_wrelu = sem("w_exponent_ready")
        s_wexp = sem("w_ready")
        s_z = sem("general_z_ready")
        s_p = sem("p_ready")
        s_hi = sem("hi_ready")
        s_lo = sem("lo_ready")
        s_t32 = sem("t_float32_ready")
        s_t16 = sem("t_pairs_ready")
        s_mm = sem("products_done")
        s_gen = sem("general_maximum_steps")
        s_xr = [sem(f"xrow_in{o}") for o in range(2)]
        s_rd = sem("reciprocal_ready")
        s_res = sem("residual_ready")
        s_quot = sem("quotient_ready")
        s_bn = sem("bn_stats_ready")
        s_mv = sem("mean_variance_ready")
        s_ve = sem("variance_eps_ready")
        s_ln = sem("log_ready")
        s_r0 = sem("rstd_guess_ready")
        s_nw = sem("newton_steps")
        s_out = sem("rows_normalised")
        s_store = [sem(f"rows_stored{o}") for o in range(2)]
        block = stack.enter_context(nc.Block())

        def wait(eng, s, v):
            if not isinstance(v, int) or v > 0:
                eng.wait_ge(s, v)

        def load_strip(eng, n, b):
            for q in range(Q):
                eng.dma_start(strip[q * B:(q + 1) * B, b, :],
                              adj[bass.ds(n * B, B), q * NQ:(q + 1) * NQ]).then_inc(s_adj[b], 16)

        @block.sync
        def _(sp):
            sp.dma_start(W, w_common.rearrange("(p h) k -> p h k", p=P)).then_inc(s_w, 16)
            for c, w in enumerate((w_right, w_left)):
                sp.dma_start(wcol[:, c, :], w.rearrange("(p h) -> p h", p=P)).then_inc(s_w, 16)
            for c, b in enumerate((b_right, b_left)):
                sp.dma_start(bias[:, c:c + 1], b.broadcast_to([P, 1])).then_inc(s_w, 16)
            cv = ctx_in.rearrange("(p t) k -> p t k", p=P)
            for c in range(NCH):
                if c >= 4:
                    sp.wait_ge(s_dot, (c - 3) * CT)
                    sp.wait_ge(s_prod, (c - 3) * CT)
                sp.dma_start(cstage[c % 4], cv[:, c * CT:(c + 1) * CT, :]).then_inc(s_ctx[c % 4], 16)
                if c == 3:
                    for q in range(Q):
                        sp.dma_start(xs[q * B:(q + 1) * B, :, :],
                                     x[q * NQ:(q + 1) * NQ, :].rearrange("(j p) d -> p j d", p=B)).then_inc(s_x, 16)
            for n in range(NB - 1):
                load_strip(sp, n, n)
            sp.wait_ge(s_v, 1)
            load_strip(sp, NB - 1, NB - 1)
            sp.wait_ge(s_lr, 2)
            sp.dma_start(lr_dram.rearrange("c (p t) -> p c t", p=P), LR[:, :, :]).then_inc(s_lrout, 16)
            sp.wait_ge(s_lrout, 16)
            for h in range(2):
                sp.dma_start(lrep[:, h, 0, :],
                             lr_dram[1, h * P * B:(h + 1) * P * B].rearrange("(s i) -> s i", i=B)).then_inc(s_tab, 16)
            sp.dma_start(rcol[:, :, :], lr_dram[0, :].rearrange("(q j p) -> j q p", q=Q, p=B)).then_inc(s_tab, 16)
            for q in range(Q):
                sp.dma_start(tab[q * B:(q + 1) * B, :],
                             lr_dram[0:1, q * NQ:(q + 1) * NQ].broadcast_to([B, NQ])).then_inc(s_tab, 16)

            def store(g, o):
                sp.wait_ge(s_out, g + 1)
                sp.dma_start(out[bass.ds(g * P, P), :], y[:, o, 0:D]).then_inc(s_store[o], 16)

            def load_xrow(g, o):
                wait(sp, s_res, g - 1)
                sp.dma_start(xrow[:, o, :], x[bass.ds(g * P, P), :]).then_inc(s_xr[o], 16)

            def steps(it, last):
                for k in range(SI):
                    n = it * SI + k
                    g = it * GI + k // SG
                    if k % SG == 1 and (not isinstance(g, int) or g >= 1):
                        load_xrow(g - 1, (k // SG + 1) % 2)
                    if not (last and k >= SI - NB):
                        sp.wait_ge(s_t32, n + 1)
                        sp.wait_ge(s_lo, n + 1)
                        load_strip(sp, n + NB, k % NB)
                    if k % SG == SG - 1 and (not isinstance(g, int) or g >= 3):
                        store(g - 3, (k // SG + 1) % 2)

            steps(0, False)
            steps(1, False)
            with sp.Fori(2, IT - 1) as it:
                steps(it, False)
            steps(IT - 1, True)
            load_xrow(NG - 1, 1)
            for g in range(NG - 3, NG):
                store(g, g % 2)
            for o in range(2):
                sp.wait_ge(s_store[o], 16 * (NG // 2))

        @block.gpsimd
        def _(pool):
            nc.gpsimd.memset(ident[:, :], 0.0).then_inc(s_id, 1)
            for c, v in enumerate((EPS, -0.5, 1.5)):
                nc.gpsimd.memset(const[:, c:c + 1], v).then_inc(s_const, 1)
            pool.wait_ge(s_id, 1)
            nc.gpsimd.affine_select(out=ident[:, :], in_=ident[:, :], compare_op=ALU.not_equal, fill=1.0, base=0,
                                    pattern=[[-1, P]], channel_multiplier=1).then_inc(s_id, 1)
            pool.wait_ge(s_psfree, 2)
            for c in range(NCH):
                pool.wait_ge(s_ctx[c % 4], 16 * (c // 4 + 1))
                for t in range(CT):
                    i = c * CT + t
                    if i >= 2:
                        pool.wait_ge(s_sum, i - 1)
                    nc.gpsimd.tensor_tensor(pair[:, i % 2, 0:CIN], cstage[c % 4][:, t, :], vb[:, 1, :],
                                            ALU.mult).then_inc(s_prod, 1)
            pool.wait_ge(s_mx, 3)
            nc.gpsimd.partition_all_reduce(amx, mx3, P, RMAX).then_inc(s_amx, 1)

            def residual(h, o):
                g = h * 2 + o
                rd, rs, ve, vh = st(0, o), st(4, o), st(3, o), st(7, o)
                pool.wait_ge(s_rd, g + 1)
                nc.gpsimd.tensor_tensor(rs, rd, pe2, ALU.mult).then_inc(s_quot, 1)
                pool.wait_ge(s_quot, g * 2 + 1)
                nc.gpsimd.tensor_tensor(y[:, o, 0:D], y[:, o, 0:D], rs.broadcast_to([P, D]),
                                        ALU.mult).then_inc(s_quot, 1)
                pool.wait_ge(s_quot, g * 2 + 2)
                pool.wait_ge(s_xr[o], h * 16 + 16)
                nc.gpsimd.tensor_tensor(y[:, o, 0:D], y[:, o, 0:D], xrow[:, o, :], ALU.add).then_inc(s_res, 1)
                pool.wait_ge(s_mv, g + 1)
                nc.gpsimd.tensor_tensor(ve, st(2, o), const[:, 0:1], ALU.add).then_inc(s_ve, 1)
                pool.wait_ge(s_ve, g + 1)
                nc.gpsimd.tensor_tensor(vh, ve, const[:, 1:2], ALU.mult).then_inc(s_half, 1)

            def normalise(h, o):
                g = h * 2 + o
                r0, t, vh = st(5, o), st(6, o), st(7, o)
                pool.wait_ge(s_r0, g + 1)
                pool.wait_ge(s_half, g + 1)
                nc.gpsimd.tensor_tensor(t, r0, r0, ALU.mult).then_inc(s_nw, 1)
                pool.wait_ge(s_nw, g * 5 + 1)
                nc.gpsimd.tensor_tensor(t, t, vh, ALU.mult).then_inc(s_nw, 1)
                pool.wait_ge(s_nw, g * 5 + 2)
                nc.gpsimd.tensor_tensor(t, t, const[:, 2:3], ALU.add).then_inc(s_nw, 1)
                pool.wait_ge(s_nw, g * 5 + 3)
                nc.gpsimd.tensor_tensor(t, t, r0, ALU.mult).then_inc(s_nw, 1)
                nc.gpsimd.tensor_tensor(y[:, o, 0:D], y[:, o, 0:D], st(1, o).broadcast_to([P, D]),
                                        ALU.subtract).then_inc(s_nw, 1)
                pool.wait_ge(s_nw, g * 5 + 5)
                nc.gpsimd.tensor_tensor(y[:, o, 0:D], y[:, o, 0:D], t.broadcast_to([P, D]),
                                        ALU.mult).then_inc(s_out, 1)

            pool.wait_ge(s_sc, 1)
            pool.wait_ge(s_const, 3)
            residual(0, 0)
            residual(0, 1)
            normalise(0, 0)
            residual(1, 0)
            normalise(0, 1)
            residual(1, 1)
            normalise(1, 0)
            with pool.Fori(2, NG // 2) as h:
                residual(h, 0)
                normalise(h - 1, 1)
                residual(h, 1)
                normalise(h, 0)
            normalise(NG // 2 - 1, 1)

        @block.tensor
        def _(pe):
            pe.wait_ge(s_w, 80)
            pe.wait_ge(s_wrep, 1)
            for c in range(2):
                for h in range(2):
                    m = nc.tensor.matmul(ps[c][:, 0:CIN], wrep[:, c, h, :], W[:, h, :], start=(h == 0), stop=(h == 1))
            m.then_inc(s_v, 1)
            pe.wait_ge(s_id, 2)
            pe.wait_ge(s_rep, 1)
            for h in range(2):
                m = nc.tensor.transpose(pt[:, h * P:(h + 1) * P], lrep[:, h, :, :].rearrange("p q i -> p (q i)"),
                                        ident[:, :])
            m.then_inc(s_lT, 1)
            nc.tensor.transpose(pt[:, NS:NS + JB], rcol[:, :, :].rearrange("j q p -> j (q p)"),
                                ident[0:JB, 0:JB]).then_inc(s_rT, 1)
            pe.wait_ge(s_xh, JB)
            pe.wait_ge(s_xrdy, JS + 3)
            with pe.Fori(0, IT) as it:
                for b in range(GI):
                    g = it * GI + b
                    pe.wait_ge(s_t32, (g + 1) * SG)
                    pe.wait_ge(s_psfree, g + 1)
                    acc = ps[b]
                    for jb in range(JS, JB):
                        nc.tensor.matmul(acc[:, 0:D + 1], T[:, b, jb, :], X[:, jb, 0:D + 1],
                                         start=(jb == JS), stop=False)
                    pe.wait_ge(s_t16, (g + 1) * SG)
                    for jb in range(JS):
                        hi, lo = T16[:, b, jb, :, 0], T16[:, b, jb, :, 1]
                        nc.tensor.matmul(acc[:, 0:D + 1], hi, X16[:, jb, 0:D + 1], start=False, stop=False)
                        nc.tensor.matmul(acc[:, 0:D + 1], hi, X16[:, jb, D + 2:2 * D + 3], start=False, stop=False)
                        m = nc.tensor.matmul(acc[:, 0:D + 1], lo, X16[:, jb, 0:D + 1], start=False,
                                             stop=(jb == JS - 1))
                    m.then_inc(s_mm, 1)

        @block.scalar
        def _(act):
            for c in range(2):
                if c == 0:
                    act.wait_ge(s_v, 1)
                nc.scalar.activation(vb[:, c, :], ps[c][:, 0:CIN], ACT.Copy).then_inc(s_psfree, 1)
            for i in range(N // P):
                act.wait_ge(s_prod, i + 1)
                nc.scalar.activation(pair[:, i % 2, 0:CIN], pair[:, i % 2, 0:CIN], ACT.Identity,
                                     accum_out=LR[:, 1, i:i + 1]).then_inc(s_sum, 1)
            act.wait_ge(s_F, 1)
            nc.scalar.activation(F[:, :], F[:, :], ACT.Exp).then_inc(s_F, 1)
            act.wait_ge(s_F, 4)
            for j in range(JB):
                dst = X16[:, j, 0:D] if j < JS else X[:, j, 0:D]
                nc.scalar.activation(dst, xs[:, j, :], ACT.Copy, scale=Fx[:, j:j + 1]).then_inc(s_xh, 1)
            act.wait_ge(s_tabs, 4)
            general = act.value_load(flag.bitcast(I32)[0:1, 0:1])

            def evacuate(g, o, half):
                act.wait_ge(s_mm, g + 1)
                wait(act, s_store[o], half * 16)
                nc.scalar.activation(y[:, o, :], ps[o][:, 0:D + 1], ACT.Relu).then_inc(s_psfree, 1)

            def guess(g, o):
                act.wait_ge(s_ve, g + 1)
                nc.scalar.activation(st(4, o), st(3, o), ACT.Ln).then_inc(s_ln, 1)
                act.wait_ge(s_ln, g + 1)
                nc.scalar.activation(st(5, o), st(4, o), ACT.Exp, scale=-0.5).then_inc(s_r0, 1)

            def weights(n, k):
                with act.If(general == 0):
                    nc.scalar.activation(w[:, k % 2, :], tab[:, :], ACT.Relu, bias=b1[:, bass.ds(n, 1)],
                                         scale=SLOPE - 1.0).then_inc(s_wrelu, 1)
                    act.wait_ge(s_wrelu, n + 1)
                    nc.scalar.activation(w[:, k % 2, :], w[:, k % 2, :], ACT.Exp,
                                         bias=b2[:, bass.ds(n, 1)]).then_inc(s_wexp, 1)
                with act.Else():
                    s = strip[:, k % NB, :]
                    act.wait_ge(s_z, n + 1)
                    nc.scalar.activation(w[:, k % 2, :], s, ACT.Exp, bias=b2[:, bass.ds(n, 1)],
                                         scale=-SLOPE * BIG).then_inc(s_wrelu, 1)
                    act.wait_ge(s_wrelu, n + 1)
                    nc.scalar.activation(s, s, ACT.Exp, bias=b1[:, bass.ds(n, 1)], scale=-BIG).then_inc(s_wexp, 1)

            def steps(it, last):
                for k in range(SI):
                    n, b, g, o = it * SI + k, k % NB, it * GI + k // SG, (k // SG) % 2
                    act.wait_ge(s_p, n + 1)
                    wait(act, s_t16, n - 1)
                    nc.scalar.activation(pair16[:, k % 2, :, 0], strip[:, b, 0:CS], ACT.Copy,
                                         scale=PSCALE).then_inc(s_hi, 1)
                    if not (last and k >= SI - 2):
                        weights(n + 2, k + 2)
                    if k % SG == 1 and (not isinstance(g, int) or g >= 2):
                        evacuate(g - 2, o, it - 1)
                    if k % SG == 3 and (not isinstance(g, int) or g >= 3):
                        guess(g - 3, 1 - o)

            weights(0, 0)
            weights(1, 1)
            steps(0, False)
            steps(1, False)
            with act.Fori(2, IT - 1) as it:
                steps(it, False)
            steps(IT - 1, True)
            for g in range(NG - 2, NG):
                evacuate(g, g % 2, g // 2)
                guess(g - 1, (g - 1) % 2)
            guess(NG - 1, (NG - 1) % 2)

        @block.vector
        def _(dve):
            dve.wait_ge(s_w, 80)
            for c in range(2):
                for h in range(2):
                    m = nc.vector.tensor_copy(wrep[:, c, h, :], wcol[:, c, h:h + 1].broadcast_to([P, P]))
            m.then_inc(s_wrep, 1)
            dve.wait_ge(s_psfree, 2)
            for c in range(NCH):
                dve.wait_ge(s_ctx[c % 4], 16 * (c // 4 + 1))
                for t in range(CT):
                    i = c * CT + t
                    if i >= 4:
                        dve.wait_ge(s_dot, i - 3)
                    nc.vector.scalar_tensor_tensor(out=tab[:, i % 4 * CIN:(i % 4 + 1) * CIN], in0=cstage[c % 4][:, t, :], scalar=1.0,
                                                   in1=vb[:, 0, :], op0=ALU.mult, op1=ALU.mult,
                                                   accum_out=LR[:, 0, i:i + 1]).then_inc(s_dot, 1)
            dve.wait_ge(s_dot, N // P)
            nc.vector.tensor_scalar(LR[:, 0, :], LR[:, 0, :], bias[:, 0:1], None, ALU.add).then_inc(s_lr, 1)
            dve.wait_ge(s_sum, N // P)
            nc.vector.tensor_scalar(LR[:, 1, :], LR[:, 1, :], bias[:, 1:2], None, ALU.add).then_inc(s_lr, 1)
            dve.wait_ge(s_lr, 2)
            nc.vector.tensor_reduce(mx3[:, 0:1], LR[:, 0, :], AX.X, ALU.max).then_inc(s_mx, 1)
            nc.vector.tensor_reduce(mnq, LR[:, 0, :], AX.X, ALU.min).then_inc(s_setup, 1)
            dve.wait_ge(s_setup, 1)
            nc.vector.tensor_scalar(mx3[:, 1:2], mnq, -1.0, None, ALU.mult).then_inc(s_mx, 1)
            dve.wait_ge(s_x, 64)
            nc.vector.tensor_reduce(mx3[:, 2:3], xs, AX.XY, ALU.max, apply_absolute_value=True).then_inc(s_mx, 1)
            dve.wait_ge(s_amx, 1)
            nc.vector.tensor_scalar(pe2.bitcast(I32), amx[:, 2:3].bitcast(I32), 0x7F800000, None,
                                    ALU.bitwise_and).then_inc(s_setup, 1)
            dve.wait_ge(s_setup, 2)
            nc.vector.tensor_scalar(pe2, pe2, 2.0 ** -100, 2.0 ** 100, ALU.max, ALU.min).then_inc(s_setup, 1)
            dve.wait_ge(s_setup, 3)
            nc.vector.tensor_scalar(inv, pe2, 2.0 ** -14, None, ALU.mult).then_inc(s_setup, 1)
            dve.wait_ge(s_setup, 4)
            nc.vector.reciprocal(sc, inv).then_inc(s_sc, 1)
            nc.vector.tensor_tensor(spread, amx[:, 0:1], amx[:, 1:2], ALU.add).then_inc(s_setup, 1)
            dve.wait_ge(s_setup, 5)
            nc.vector.tensor_scalar(flag.bitcast(I32), spread, SPREAD, None, ALU.is_gt).then_inc(s_setup, 1)
            nc.vector.tensor_scalar(flagf, spread, SPREAD, None, ALU.is_gt).then_inc(s_setup, 1)
            dve.wait_ge(s_setup, 7)
            nc.vector.tensor_scalar(fast, flagf, -1.0, 1.0, ALU.mult, ALU.add).then_inc(s_setup, 1)
            dve.wait_ge(s_setup, 8)
            nc.vector.scalar_tensor_tensor(out=tscale, in0=flagf, scalar=-1.0 / BIG, in1=fast, op0=ALU.mult,
                                           op1=ALU.add).then_inc(s_setup, 1)
            dve.wait_ge(s_tab, 112)
            for q in range(1, Q):
                m = nc.vector.tensor_copy(lrep[:, :, q, :], lrep[:, :, 0, :])
            m.then_inc(s_rep, 1)
            dve.wait_ge(s_rT, 1)
            nc.vector.tensor_scalar(F[:, :], pt[:, NS:NS + JB], amx[:, 0:1], fast, ALU.subtract,
                                    ALU.mult).then_inc(s_F, 1)
            dve.wait_ge(s_F, 2)
            nc.vector.tensor_scalar(Fx[:, 0:JS], F[:, 0:JS], sc, None, ALU.mult).then_inc(s_F, 1)
            nc.vector.tensor_scalar(Fx[:, JS:JB], F[:, JS:JB], sc, PSCALE, ALU.mult, ALU.mult).then_inc(s_F, 1)
            dve.wait_ge(s_setup, 9)
            nc.vector.tensor_scalar(tab[:, :], tab[:, :], amx[:, 0:1], tscale, ALU.subtract,
                                    ALU.mult).then_inc(s_tabs, 1)
            dve.wait_ge(s_lT, 1)
            nc.vector.tensor_scalar(lb[:, :], pt[:, 0:NS], amx[:, 0:1], None, ALU.add).then_inc(s_tabs, 1)
            dve.wait_ge(s_tabs, 2)
            nc.vector.tensor_scalar(b1[:, :], lb[:, :], SLOPE - 1.0, None, ALU.mult).then_inc(s_tabs, 1)
            dve.wait_ge(s_tabs, 3)
            nc.vector.tensor_scalar(b2[:, :], lb[:, :], spread, 1.0 - SLOPE, ALU.subtract,
                                    ALU.mult).then_inc(s_setup, 1)
            dve.wait_ge(s_setup, 10)
            nc.vector.tensor_scalar(b2[:, :], b2[:, :], 0.0, None, ALU.min).then_inc(s_tabs, 1)
            nc.vector.tensor_scalar(X16[:, 0:JS, D], F[:, 0:JS], FSCALE, None, ALU.mult).then_inc(s_xrdy, 1)
            nc.vector.tensor_scalar(X[:, JS:JB, D], F[:, JS:JB], FSCALE * PSCALE, None, ALU.mult).then_inc(s_xrdy, 1)
            dve.wait_ge(s_xrdy, 1)
            nc.vector.scalar_tensor_tensor(out=X16[:, 0:JS, 2 * D + 2], in0=F[:, 0:JS], scalar=FSCALE,
                                           in1=X16[:, 0:JS, D], op0=ALU.mult, op1=ALU.subtract).then_inc(s_xrdy, 1)
            for j in range(JS):
                dve.wait_ge(s_xh, j + 1)
                nc.vector.scalar_tensor_tensor(out=X16[:, j, D + 2:2 * D + 2], in0=xs[:, j, :], scalar=Fx[:, j:j + 1],
                                               in1=X16[:, j, 0:D], op0=ALU.mult,
                                               op1=ALU.subtract).then_inc(s_xrdy, 1)
            dve.wait_ge(s_xh, JB)
            dve.wait_ge(s_xrdy, JS + 3)
            dve.wait_ge(s_tabs, 4)
            general = dve.value_load(flag.bitcast(I32)[0:1, 0:1])

            def masked(n, b, k, use):
                s = strip[:, b, :]
                with dve.If(general == 0):
                    dve.wait_ge(s_adj[b], use * 16 * Q)
                    dve.wait_ge(s_wexp, n + 1)
                    nc.vector.scalar_tensor_tensor(out=s, in0=s, scalar=0.0, in1=w[:, k % 2, :], op0=ALU.is_gt,
                                                   op1=ALU.mult).then_inc(s_p, 1)
                with dve.Else():
                    dve.wait_ge(s_adj[b], use * 16 * Q)
                    step = [0]

                    def chain(m):
                        m.then_inc(s_gen, 1)
                        step[0] += 1
                        dve.wait_ge(s_gen, n * GEN + step[0])

                    chain(nc.vector.scalar_tensor_tensor(out=s, in0=s, scalar=0.0, in1=tab[:, :], op0=ALU.is_le,
                                                         op1=ALU.max))
                    chain(nc.vector.tensor_reduce(mnq, s, AX.X, ALU.min))
                    for q in range(Q):
                        chain(nc.vector.tensor_copy(c4[0:B, q:q + 1], mnq[q * B:(q + 1) * B, :]))
                    chain(nc.vector.tensor_reduce(m1[0:B, :], c4[0:B, :], AX.X, ALU.min))
                    for q in range(Q):
                        chain(nc.vector.tensor_copy(mn[q * B:(q + 1) * B, :], m1[0:B, :]))
                    lbn = lb[:, bass.ds(n, 1)]
                    chain(nc.vector.scalar_tensor_tensor(out=mnq, in0=mn, scalar=-BIG, in1=lbn, op0=ALU.mult,
                                                         op1=ALU.add))
                    chain(nc.vector.scalar_tensor_tensor(out=mn, in0=mnq, scalar=SLOPE, in1=mnq, op0=ALU.mult,
                                                         op1=ALU.max))
                    chain(nc.vector.tensor_scalar(nmax, mn, FLOOR, -1.0, ALU.max, ALU.mult))
                    chain(nc.vector.tensor_tensor(b1[:, bass.ds(n, 1)], lbn, nmax, ALU.add))
                    assert step[0] == GEN
                    nc.vector.scalar_tensor_tensor(out=b2[:, bass.ds(n, 1)], in0=lbn, scalar=SLOPE, in1=nmax,
                                                   op0=ALU.mult, op1=ALU.add).then_inc(s_z, 1)
                    dve.wait_ge(s_wexp, n + 1)
                    nc.vector.tensor_tensor(s, s, w[:, k % 2, :], ALU.max).then_inc(s_p, 1)

            def reciprocal(g, o):
                dve.wait_ge(s_psfree, g + 3)
                nc.vector.reciprocal(st(0, o), y[:, o, D:D + 1]).then_inc(s_rd, 1)

            def moments(g, o):
                dve.wait_ge(s_res, g + 1)
                nc.vector.bn_stats(small[:, 28 + 14 * o + 8:28 + 14 * o + 14], y[:, o, 0:D]).then_inc(s_bn, 1)
                dve.wait_ge(s_tabs, 2)
                dve.wait_ge(s_bn, g + 1)
                nc.vector.bn_aggr(small[:, 28 + 14 * o + 1:28 + 14 * o + 3],
                                  small[:, 28 + 14 * o + 8:28 + 14 * o + 14]).then_inc(s_mv, 1)

            def steps(it, last):
                for k in range(SI):
                    n, b, g, o = it * SI + k, k % NB, it * GI + k // SG, (k // SG) % 2
                    s0 = (k % SG) * B
                    if not (last and k == SI - 1):
                        use = (it * SI + k + 1) // NB + 1 if isinstance(it, int) else it * (SI // NB) + (k + 1) // NB + 1
                        masked(n + 1, (k + 1) % NB, k + 1, use)
                    dve.wait_ge(s_p, n + 1)
                    if k % SG == 0:
                        wait(dve, s_mm, g - 1)
                    nc.vector.transpose(T[:, o, JS:JB, s0:s0 + B],
                                        strip[:, b, CS:NQ].rearrange("p (j i) -> p j i", i=B)).then_inc(s_t32, 1)
                    dve.wait_ge(s_hi, n + 1)
                    nc.vector.scalar_tensor_tensor(out=pair16[:, k % 2, :, 1], in0=strip[:, b, 0:CS], scalar=PSCALE,
                                                   in1=pair16[:, k % 2, :, 0], op0=ALU.mult,
                                                   op1=ALU.subtract).then_inc(s_lo, 1)
                    dve.wait_ge(s_lo, n + 1)
                    nc.vector.transpose(T[:, o, 0:JS, s0:s0 + B],
                                        pair[:, k % 2, :].rearrange("p (j i) -> p j i", i=B)).then_inc(s_t16, 1)
                    if k % SG == 2 and (not isinstance(g, int) or g >= 2):
                        reciprocal(g - 2, o)
                    if k % SG == 3 and (not isinstance(g, int) or g >= 2):
                        moments(g - 2, o)

            masked(0, 0, 0, 1)
            steps(0, False)
            with dve.Fori(1, IT - 1) as it:
                steps(it, False)
            steps(IT - 1, True)
            for g in range(NG - 2, NG):
                reciprocal(g, g % 2)
                moments(g, g % 2)


_INS = ["x", "adj", "L0_gnn_context", "L0_gnn_W_common", "L0_gnn_w_left", "L0_gnn_b_left", "L0_gnn_w_right",
        "L0_gnn_b_right"]


def kernel(**inputs):
    import numpy as _np
    import concourse.bacc as _bacc
    from concourse import mybir as _mybir
    from concourse.bass_utils import run_bass_kernel_spmd as _run

    nc = _bacc.Bacc("TRN2", target_bir_lowering=False, num_devices=1)
    arrays, args = {}, []
    for name in _INS:
        a = _np.ascontiguousarray(inputs[name])
        if a.ndim == 0:
            a = a.reshape(1)
        arrays[f"in_{name}_dram"] = a
        args.append(nc.dram_tensor(f"in_{name}_dram", a.shape, _mybir.dt.from_np(a.dtype), kind="ExternalInput").ap())
    shape = inputs["x"].shape
    args.append(nc.dram_tensor("out_dram", shape, _mybir.dt.float32, kind="ExternalOutput").ap())
    build(nc, *args)
    r = _run(nc, [arrays], core_ids=[0])
    return r.results[0]["out_dram"]
```

```python
import math

import concourse.bass as bass
from concourse import mybir
from contextlib import ExitStack

F32 = mybir.dt.float32
F16 = mybir.dt.float16
I32 = mybir.dt.int32
ALU = mybir.AluOpType
ACT = mybir.ActivationFunctionType
AX = mybir.AxisListType
RMAX = bass.bass_isa.ReduceOp.max


def build(nc, x, adj, ctx_in, w_common, w_left, b_left, w_right, b_right, out):
    N, D = x.shape
    CIN = ctx_in.shape[1]
    HID = w_common.shape[0]
    P = 128
    Q = 4
    B = P // Q
    NQ = N // Q
    JB = NQ // B
    NS = N // B
    SG = P // B
    NG = N // P
    JS = 38
    CS = JS * B
    XW = D + 2
    NB = 4
    GI = 2
    SI = GI * SG
    IT = NG // GI
    NT = N // P
    OWN = [i for i in range(NT) if i * 9 % 32 >= 23]
    CT = 8
    NCH = N // P // CT
    XC = JB // 4
    NEWTON = 3
    BIG = 2.0 ** 100
    PSCALE = 2.0 ** 15
    SPREAD = 10.0
    SLOPE = 0.2
    EPS = 1e-5
    GUESS = 0.5 * math.log(2.0) * (127 - 0.043)
    FLOOR = -1e28
    GEN = 15
    FSCALE = 2.0 ** 14

    stack = ExitStack()
    with stack:
        def sb(name, shape, dt=F32):
            return stack.enter_context(nc.sbuf_tensor(name, shape, dt))

        def sem(name):
            return stack.enter_context(nc.semaphore(name))

        X = sb("X", [P, JB, XW])
        T = sb("T", [P, 2, JB, P])
        strip = sb("strip", [P, NB, NQ])
        pair = sb("pair", [P, 2, CS])
        w = sb("w", [P, 2, NQ])
        tab = sb("tab", [P, NQ])
        lb = sb("lb", [P, NS])
        b1 = sb("b1", [P, NS])
        b2 = sb("b2", [P, NS])
        xrow = sb("xrow", [P, 2, D])
        y = sb("y", [P, 2, D + 1])
        ident = sb("ident", [P, P])
        small = sb("small", [P, 64])
        const = sb("const", [P, 4])
        LR = sb("LR", [P, 2, JB])
        lrep = sb("lrep", [P, 2, Q, B])
        rcol = sb("rcol", [JB, Q, B])
        F = sb("F", [P, JB])
        Fx = sb("Fx", [P, JB])
        wcol = sb("wcol", [P, 2, HID // P])
        bias = sb("bias", [P, 2])
        W = strip[:, 3, 0:2 * CIN].rearrange("p (h k) -> p h k", h=2)
        wrep = strip[:, 3, 2 * CIN:2 * CIN + 4 * P].rearrange("p (c h m) -> p c h m", c=2, h=2)
        vb = w[:, 0, 0:2 * CIN].rearrange("p (c k) -> p c k", c=2)
        xs = T[:, :, :, :].rearrange("p b j m -> p (b j m)").rearrange("p (j d) -> p j d", d=D)
        Xflat = X[:, :, :].rearrange("p j w -> p (j w)")
        X16 = Xflat.bitcast(F16).rearrange("p (j w) -> p j w", w=2 * XW)
        T16 = T[:, :, :, :].rearrange("p b j m -> p (b j m)").bitcast(F16).rearrange(
            "p (b j m e) -> p b j m e", b=2, j=JB, e=2)
        pair16 = pair[:, :, :].rearrange("p b c -> p (b c)").bitcast(F16).rearrange(
            "p (b c e) -> p b c e", b=2, e=2)
        cstage = [Xflat[:, s * CT * CIN:(s + 1) * CT * CIN].rearrange("p (t k) -> p t k", k=CIN) for s in range(4)]

        mx3, amx = small[:, 0:3], small[:, 4:7]
        pe2, inv, sc = small[:, 8:9], small[:, 9:10], small[:, 10:11]
        spread = small[:, 11:12]
        flag = small[:, 12:13]
        flagf, fast, tscale = small[:, 13:14], small[:, 14:15], small[:, 15:16]
        neg_spread = small[:, 24:25]
        mnq, m1, mn = small[:, 16:17], small[:, 17:18], small[:, 18:19]
        mxx = small[:, 56:60]
        c4 = small[:, 20:24]
        nmax = small[:, 19:20]

        def st(name_col, o):
            return small[:, 28 + 14 * o + name_col:29 + 14 * o + name_col]

        ps = [stack.enter_context(nc.psum_tensor(f"ps{i}", [P, 512], F32)) for i in range(2)]
        pt = stack.enter_context(nc.psum_tensor("pt", [P, 512], F32))
        lr_dram = nc.dram_tensor("lr_scratch", [2, N], F32, kind="Internal").ap()

        s_mxx = sem("x_maxima_ready")
        s_x32 = sem("x_float32_operands_ready")
        s_const = sem("constants_ready")
        s_half = sem("half_variance_ready")
        s_w = sem("weights_in")
        s_ctx = [sem(f"context_in{s}") for s in range(4)]
        s_x = [sem(f"x_in{c}") for c in range(4)]
        s_wrep = sem("w_replicated")
        s_v = sem("v_ready")
        s_psfree = sem("psum_evacuated")
        s_prod = sem("product_ready")
        s_sum = sem("product_summed")
        s_dot = sem("right_dots_done")
        s_lr = sem("left_right_ready")
        s_lrout = sem("left_right_stored")
        s_tab = sem("tables_in")
        s_mx = sem("partial_maxima")
        s_amx = sem("overall_maxima")
        s_id = sem("identity_ready")
        s_rep = sem("left_replicated")
        s_lT = sem("left_transposed")
        s_sc = sem("x_scale_ready")
        s_xh = sem("x_high_ready")
        s_tabs = sem("bias_tables_ready")
        s_xrdy = sem("x_low_and_ones_ready")
        s_setup = sem("vector_setup_steps")
        s_adj = [sem(f"adj_in{b}") for b in range(NB)]
        s_rT = sem("right_transposed")
        s_F = sem("factor_steps")
        s_wrelu = sem("w_exponent_ready")
        s_wexp = sem("w_ready")
        s_z = sem("general_z_ready")
        s_p = sem("p_ready")
        s_hi = sem("hi_ready")
        s_lo = sem("lo_ready")
        s_t32 = sem("t_float32_ready")
        s_t16 = sem("t_pairs_ready")
        s_mm = sem("products_done")
        s_gen = sem("general_maximum_steps")
        s_xr = [sem(f"xrow_in{o}") for o in range(2)]
        s_rd = sem("reciprocal_ready")
        s_res = sem("residual_ready")
        s_quot = sem("quotient_ready")
        s_bn = sem("bn_stats_ready")
        s_mv = sem("mean_variance_ready")
        s_ve = sem("variance_eps_ready")
        s_r0 = sem("rstd_guess_ready")
        s_nw = sem("newton_steps")
        s_out = sem("rows_normalised")
        s_store = [sem(f"rows_stored{o}") for o in range(2)]
        block = stack.enter_context(nc.Block())

        def wait(eng, s, v):
            if not isinstance(v, int) or v > 0:
                eng.wait_ge(s, v)

        def load_strip(eng, n, b):
            for q in range(Q):
                eng.dma_start(strip[q * B:(q + 1) * B, b, :],
                              adj[bass.ds(n * B, B), q * NQ:(q + 1) * NQ]).then_inc(s_adj[b], 16)

        @block.sync
        def _(sp):
            sp.dma_start(W, w_common.rearrange("(p h) k -> p h k", p=P)).then_inc(s_w, 16)
            for c, w in enumerate((w_right, w_left)):
                sp.dma_start(wcol[:, c, :], w.rearrange("(p h) -> p h", p=P)).then_inc(s_w, 16)
            for c, b in enumerate((b_right, b_left)):
                sp.dma_start(bias[:, c:c + 1], b.broadcast_to([P, 1])).then_inc(s_w, 16)
            cv = ctx_in.rearrange("(p t) k -> p t k", p=P)
            def load_x(c):
                for q in range(Q):
                    r0 = q * NQ + c * XC * B
                    sp.dma_start(xs[q * B:(q + 1) * B, c * XC:(c + 1) * XC, :],
                                 x[r0:r0 + XC * B, :].rearrange("(j p) d -> p j d", p=B)).then_inc(s_x[c], 16)

            load_x(0)
            for c in range(NCH):
                if c >= 4:
                    end = (c - 3) * CT
                    own = sum(i < end for i in OWN)
                    sp.wait_ge(s_dot, end + own)
                    sp.wait_ge(s_prod, end - own)
                sp.dma_start(cstage[c % 4], cv[:, c * CT:(c + 1) * CT, :]).then_inc(s_ctx[c % 4], 16)
                if 0 < c < 4:
                    load_x(c)
            for n in range(NB - 1):
                load_strip(sp, n, n)
            sp.wait_ge(s_v, 1)
            load_strip(sp, NB - 1, NB - 1)
            sp.wait_ge(s_lr, 2)
            sp.dma_start(lr_dram.rearrange("c (p t) -> p c t", p=P), LR[:, :, :]).then_inc(s_lrout, 16)
            sp.wait_ge(s_lrout, 16)
            for h in range(2):
                sp.dma_start(lrep[:, h, 0, :],
                             lr_dram[1, h * P * B:(h + 1) * P * B].rearrange("(s i) -> s i", i=B)).then_inc(s_tab, 16)
            sp.dma_start(rcol[:, :, :], lr_dram[0, :].rearrange("(q j p) -> j q p", q=Q, p=B)).then_inc(s_tab, 16)
            for q in range(Q):
                sp.dma_start(tab[q * B:(q + 1) * B, :],
                             lr_dram[0:1, q * NQ:(q + 1) * NQ].broadcast_to([B, NQ])).then_inc(s_tab, 16)

            def store(g, o):
                sp.wait_ge(s_out, g + 1)
                sp.dma_start(out[bass.ds(g * P, P), :], y[:, o, 0:D]).then_inc(s_store[o], 16)

            def load_xrow(g, o):
                wait(sp, s_res, g - 1)
                sp.dma_start(xrow[:, o, :], x[bass.ds(g * P, P), :]).then_inc(s_xr[o], 16)

            def steps(it, last):
                for k in range(SI):
                    n = it * SI + k
                    g = it * GI + k // SG
                    if k % SG == 1 and (not isinstance(g, int) or g >= 1):
                        load_xrow(g - 1, (k // SG + 1) % 2)
                    if not (last and k >= SI - NB):
                        sp.wait_ge(s_t32, n + 1)
                        sp.wait_ge(s_lo, n + 1)
                        load_strip(sp, n + NB, k % NB)
                    if k % SG == SG - 1 and (not isinstance(g, int) or g >= 3):
                        store(g - 3, (k // SG + 1) % 2)

            steps(0, False)
            steps(1, False)
            with sp.Fori(2, IT - 1) as it:
                steps(it, False)
            steps(IT - 1, True)
            load_xrow(NG - 1, 1)
            for g in range(NG - 3, NG):
                store(g, g % 2)
            for o in range(2):
                sp.wait_ge(s_store[o], 16 * (NG // 2))

        @block.gpsimd
        def _(pool):
            nc.gpsimd.memset(ident[:, :], 0.0).then_inc(s_id, 1)
            for c, v in enumerate((EPS, -0.5, 1.5, GUESS)):
                nc.gpsimd.memset(const[:, c:c + 1], v).then_inc(s_const, 1)
            pool.wait_ge(s_id, 1)
            nc.gpsimd.affine_select(out=ident[:, :], in_=ident[:, :], compare_op=ALU.not_equal, fill=1.0, base=0,
                                    pattern=[[-1, P]], channel_multiplier=1).then_inc(s_id, 1)
            pool.wait_ge(s_psfree, 2)
            for c in range(NCH):
                pool.wait_ge(s_ctx[c % 4], 16 * (c // 4 + 1))
                for t in range(CT):
                    i = c * CT + t
                    if i in OWN:
                        continue
                    m = i - sum(k < i for k in OWN)
                    if m >= 2:
                        pool.wait_ge(s_sum, m - 1)
                    nc.gpsimd.tensor_tensor(pair[:, m % 2, 0:CIN], cstage[c % 4][:, t, :], vb[:, 1, :],
                                            ALU.mult).then_inc(s_prod, 1)
            pool.wait_ge(s_mx, 3)
            nc.gpsimd.partition_all_reduce(amx, mx3, P, RMAX).then_inc(s_amx, 1)

            def residual(h, o):
                g = h * 2 + o
                rd, rs, ve, vh = st(0, o), st(4, o), st(3, o), st(7, o)
                pool.wait_ge(s_rd, g + 1)
                nc.gpsimd.tensor_tensor(rs, rd, pe2, ALU.mult).then_inc(s_quot, 1)
                pool.wait_ge(s_quot, g * 2 + 1)
                nc.gpsimd.tensor_tensor(y[:, o, 0:D], y[:, o, 0:D], rs.broadcast_to([P, D]),
                                        ALU.mult).then_inc(s_quot, 1)
                pool.wait_ge(s_quot, g * 2 + 2)
                pool.wait_ge(s_xr[o], h * 16 + 16)
                nc.gpsimd.tensor_tensor(y[:, o, 0:D], y[:, o, 0:D], xrow[:, o, :], ALU.add).then_inc(s_res, 1)
                pool.wait_ge(s_mv, g + 1)
                nc.gpsimd.tensor_tensor(ve, st(2, o), const[:, 0:1], ALU.add).then_inc(s_ve, 1)
                pool.wait_ge(s_ve, g + 1)
                nc.gpsimd.tensor_tensor(vh, ve, const[:, 1:2], ALU.mult).then_inc(s_half, 1)

            def normalise(h, o):
                g = h * 2 + o
                r, t, vh = st(5, o), st(6, o), st(7, o)
                pool.wait_ge(s_r0, g + 1)
                pool.wait_ge(s_half, g + 1)
                nc.gpsimd.tensor_tensor(y[:, o, 0:D], y[:, o, 0:D], st(1, o).broadcast_to([P, D]),
                                        ALU.subtract).then_inc(s_nw, 1)
                done = 1
                for _ in range(NEWTON):
                    for out_, a_, b_, op in ((t, r, r, ALU.mult), (t, t, vh, ALU.mult), (t, t, const[:, 2:3], ALU.add),
                                             (r, r, t, ALU.mult)):
                        nc.gpsimd.tensor_tensor(out_, a_, b_, op).then_inc(s_nw, 1)
                        done += 1
                        pool.wait_ge(s_nw, g * (4 * NEWTON + 1) + done)
                nc.gpsimd.tensor_tensor(y[:, o, 0:D], y[:, o, 0:D], r.broadcast_to([P, D]),
                                        ALU.mult).then_inc(s_out, 1)

            for c in range(4):
                pool.wait_ge(s_x[c], 64)
            pool.wait_ge(s_F, 4)
            nc.gpsimd.tensor_tensor(X[:, JS:JB, 0:D], xs[:, JS:JB, :],
                                    Fx[:, JS:JB].rearrange("p (j o) -> p j o", o=1).broadcast_to([P, JB - JS, D]),
                                    ALU.mult).then_inc(s_x32, 1)
            pool.wait_ge(s_sc, 1)
            pool.wait_ge(s_const, 4)
            residual(0, 0)
            residual(0, 1)
            normalise(0, 0)
            residual(1, 0)
            normalise(0, 1)
            residual(1, 1)
            normalise(1, 0)
            with pool.Fori(2, NG // 2) as h:
                residual(h, 0)
                normalise(h - 1, 1)
                residual(h, 1)
                normalise(h, 0)
            normalise(NG // 2 - 1, 1)

        @block.tensor
        def _(pe):
            pe.wait_ge(s_w, 80)
            pe.wait_ge(s_wrep, 1)
            for c in range(2):
                for h in range(2):
                    m = nc.tensor.matmul(ps[c][:, 0:CIN], wrep[:, c, h, :], W[:, h, :], start=(h == 0), stop=(h == 1))
            m.then_inc(s_v, 1)
            pe.wait_ge(s_id, 2)
            pe.wait_ge(s_rep, 1)
            for h in range(2):
                m = nc.tensor.transpose(pt[:, h * P:(h + 1) * P], lrep[:, h, :, :].rearrange("p q i -> p (q i)"),
                                        ident[:, :])
            m.then_inc(s_lT, 1)
            nc.tensor.transpose(pt[:, NS:NS + JB], rcol[:, :, :].rearrange("j q p -> j (q p)"),
                                ident[0:JB, 0:JB]).then_inc(s_rT, 1)
            pe.wait_ge(s_xh, JS)
            pe.wait_ge(s_x32, 1)
            pe.wait_ge(s_xrdy, JS + 3)
            with pe.Fori(0, IT) as it:
                for b in range(GI):
                    g = it * GI + b
                    pe.wait_ge(s_t32, (g + 1) * SG)
                    pe.wait_ge(s_psfree, g + 1)
                    acc = ps[b]
                    for jb in range(JS, JB):
                        nc.tensor.matmul(acc[:, 0:D + 1], T[:, b, jb, :], X[:, jb, 0:D + 1],
                                         start=(jb == JS), stop=False)
                    pe.wait_ge(s_t16, (g + 1) * SG)
                    for jb in range(JS):
                        hi, lo = T16[:, b, jb, :, 0], T16[:, b, jb, :, 1]
                        nc.tensor.matmul(acc[:, 0:D + 1], hi, X16[:, jb, 0:D + 1], start=False, stop=False)
                        nc.tensor.matmul(acc[:, 0:D + 1], hi, X16[:, jb, D + 2:2 * D + 3], start=False, stop=False)
                        m = nc.tensor.matmul(acc[:, 0:D + 1], lo, X16[:, jb, 0:D + 1], start=False,
                                             stop=(jb == JS - 1))
                    m.then_inc(s_mm, 1)

        @block.scalar
        def _(act):
            for c in range(2):
                if c == 0:
                    act.wait_ge(s_v, 1)
                nc.scalar.activation(vb[:, c, :], ps[c][:, 0:CIN], ACT.Copy).then_inc(s_psfree, 1)
            for m, i in enumerate(i for i in range(NT) if i not in OWN):
                act.wait_ge(s_prod, m + 1)
                nc.scalar.activation(pair[:, m % 2, 0:CIN], pair[:, m % 2, 0:CIN], ACT.Identity,
                                     accum_out=LR[:, 1, i:i + 1]).then_inc(s_sum, 1)
            act.wait_ge(s_F, 1)
            nc.scalar.activation(F[:, :], F[:, :], ACT.Exp).then_inc(s_F, 1)
            act.wait_ge(s_F, 4)
            for c in range(4):
                act.wait_ge(s_x[c], 64)
            for j in range(JS):
                nc.scalar.activation(X16[:, j, 0:D], xs[:, j, :], ACT.Copy, scale=Fx[:, j:j + 1]).then_inc(s_xh, 1)
            act.wait_ge(s_tabs, 4)
            general = act.value_load(flag.bitcast(I32)[0:1, 0:1])

            def evacuate(g, o, half):
                act.wait_ge(s_mm, g + 1)
                wait(act, s_store[o], half * 16)
                nc.scalar.activation(y[:, o, :], ps[o][:, 0:D + 1], ACT.Relu).then_inc(s_psfree, 1)

            def guess(g, o):
                act.wait_ge(s_ve, g + 1)
                nc.scalar.activation(st(5, o), st(3, o).bitcast(I32), ACT.Exp, scale=-0.5 * math.log(2.0) / 2 ** 23,
                                     bias=const[:, 3:4]).then_inc(s_r0, 1)

            def weights(n, k):
                with act.If(general == 0):
                    nc.scalar.activation(w[:, k % 2, :], tab[:, :], ACT.Relu, bias=b1[:, bass.ds(n, 1)],
                                         scale=SLOPE - 1.0).then_inc(s_wrelu, 1)
                    act.wait_ge(s_wrelu, n + 1)
                    nc.scalar.activation(w[:, k % 2, :], w[:, k % 2, :], ACT.Exp,
                                         bias=b2[:, bass.ds(n, 1)]).then_inc(s_wexp, 1)
                with act.Else():
                    s = strip[:, k % NB, :]
                    act.wait_ge(s_z, n + 1)
                    nc.scalar.activation(w[:, k % 2, :], s, ACT.Exp, bias=b2[:, bass.ds(n, 1)],
                                         scale=-SLOPE * BIG).then_inc(s_wrelu, 1)
                    act.wait_ge(s_wrelu, n + 1)
                    nc.scalar.activation(s, s, ACT.Exp, bias=b1[:, bass.ds(n, 1)], scale=-BIG).then_inc(s_wexp, 1)

            def steps(it, last):
                for k in range(SI):
                    n, b, g, o = it * SI + k, k % NB, it * GI + k // SG, (k // SG) % 2
                    act.wait_ge(s_p, n + 1)
                    wait(act, s_t16, n - 1)
                    nc.scalar.activation(pair16[:, k % 2, :, 0], strip[:, b, 0:CS], ACT.Copy,
                                         scale=PSCALE).then_inc(s_hi, 1)
                    if not (last and k >= SI - 2):
                        weights(n + 2, k + 2)
                    if k % SG == 1 and (not isinstance(g, int) or g >= 2):
                        evacuate(g - 2, o, it - 1)
                    if k % SG == 3 and (not isinstance(g, int) or g >= 3):
                        guess(g - 3, 1 - o)

            weights(0, 0)
            weights(1, 1)
            steps(0, False)
            steps(1, False)
            with act.Fori(2, IT - 1) as it:
                steps(it, False)
            steps(IT - 1, True)
            for g in range(NG - 2, NG):
                evacuate(g, g % 2, g // 2)
                guess(g - 1, (g - 1) % 2)
            guess(NG - 1, (NG - 1) % 2)

        @block.vector
        def _(dve):
            dve.wait_ge(s_w, 80)
            for c in range(2):
                for h in range(2):
                    m = nc.vector.tensor_copy(wrep[:, c, h, :], wcol[:, c, h:h + 1].broadcast_to([P, P]))
            m.then_inc(s_wrep, 1)
            dve.wait_ge(s_x[0], 64)
            nc.vector.tensor_reduce(mxx[:, 0:1], xs[:, 0:XC, :], AX.XY, ALU.max,
                                    apply_absolute_value=True).then_inc(s_mxx, 1)
            dve.wait_ge(s_psfree, 2)
            dots = 0
            for c in range(NCH):
                dve.wait_ge(s_ctx[c % 4], 16 * (c // 4 + 1))
                for t in range(CT):
                    i = c * CT + t
                    for side in ((0, 1) if i in OWN else (0,)):
                        if dots >= 4:
                            dve.wait_ge(s_dot, dots - 3)
                        junk = dots % 4
                        nc.vector.scalar_tensor_tensor(out=tab[:, junk * CIN:(junk + 1) * CIN],
                                                       in0=cstage[c % 4][:, t, :], scalar=1.0, in1=vb[:, side, :],
                                                       op0=ALU.mult, op1=ALU.mult,
                                                       accum_out=LR[:, side, i:i + 1]).then_inc(s_dot, 1)
                        dots += 1
                if 0 < c < 4:
                    dve.wait_ge(s_x[c], 64)
                    nc.vector.tensor_reduce(mxx[:, c:c + 1], xs[:, c * XC:(c + 1) * XC, :], AX.XY, ALU.max,
                                            apply_absolute_value=True).then_inc(s_mxx, 1)
            dve.wait_ge(s_dot, dots)
            nc.vector.tensor_scalar(LR[:, 0, :], LR[:, 0, :], bias[:, 0:1], None, ALU.add).then_inc(s_lr, 1)
            dve.wait_ge(s_sum, NT - len(OWN))
            nc.vector.tensor_scalar(LR[:, 1, :], LR[:, 1, :], bias[:, 1:2], None, ALU.add).then_inc(s_lr, 1)
            dve.wait_ge(s_lr, 2)
            nc.vector.tensor_reduce(mx3[:, 0:1], LR[:, 0, :], AX.X, ALU.max).then_inc(s_mx, 1)
            nc.vector.tensor_reduce(mnq, LR[:, 0, :], AX.X, ALU.min).then_inc(s_setup, 1)
            dve.wait_ge(s_setup, 1)
            nc.vector.tensor_scalar(mx3[:, 1:2], mnq, -1.0, None, ALU.mult).then_inc(s_mx, 1)
            dve.wait_ge(s_mxx, 4)
            nc.vector.tensor_reduce(mx3[:, 2:3], mxx, AX.X, ALU.max).then_inc(s_mx, 1)
            dve.wait_ge(s_amx, 1)
            nc.vector.tensor_scalar(pe2.bitcast(I32), amx[:, 2:3].bitcast(I32), 0x7F800000, None,
                                    ALU.bitwise_and).then_inc(s_setup, 1)
            dve.wait_ge(s_setup, 2)
            nc.vector.tensor_scalar(pe2, pe2, 2.0 ** -100, 2.0 ** 100, ALU.max, ALU.min).then_inc(s_setup, 1)
            dve.wait_ge(s_setup, 3)
            nc.vector.tensor_scalar(inv, pe2, 2.0 ** -14, None, ALU.mult).then_inc(s_setup, 1)
            dve.wait_ge(s_setup, 4)
            nc.vector.reciprocal(sc, inv).then_inc(s_sc, 1)
            nc.vector.tensor_tensor(spread, amx[:, 0:1], amx[:, 1:2], ALU.add).then_inc(s_setup, 1)
            dve.wait_ge(s_setup, 5)
            nc.vector.tensor_scalar(flag.bitcast(I32), spread, SPREAD, None, ALU.is_gt).then_inc(s_setup, 1)
            nc.vector.tensor_scalar(flagf, spread, SPREAD, None, ALU.is_gt).then_inc(s_setup, 1)
            dve.wait_ge(s_setup, 7)
            nc.vector.tensor_scalar(fast, flagf, -1.0, 1.0, ALU.mult, ALU.add).then_inc(s_setup, 1)
            dve.wait_ge(s_setup, 8)
            nc.vector.scalar_tensor_tensor(out=tscale, in0=flagf, scalar=-1.0 / BIG, in1=fast, op0=ALU.mult,
                                           op1=ALU.add).then_inc(s_setup, 1)
            dve.wait_ge(s_tab, 112)
            for q in range(1, Q):
                m = nc.vector.tensor_copy(lrep[:, :, q, :], lrep[:, :, 0, :])
            m.then_inc(s_rep, 1)
            dve.wait_ge(s_rT, 1)
            nc.vector.tensor_scalar(F[:, :], pt[:, NS:NS + JB], amx[:, 0:1], fast, ALU.subtract,
                                    ALU.mult).then_inc(s_F, 1)
            dve.wait_ge(s_F, 2)
            nc.vector.tensor_scalar(Fx[:, 0:JS], F[:, 0:JS], sc, None, ALU.mult).then_inc(s_F, 1)
            nc.vector.tensor_scalar(Fx[:, JS:JB], F[:, JS:JB], sc, PSCALE, ALU.mult, ALU.mult).then_inc(s_F, 1)
            dve.wait_ge(s_setup, 9)
            nc.vector.tensor_scalar(tab[:, :], tab[:, :], amx[:, 0:1], tscale, ALU.subtract,
                                    ALU.mult).then_inc(s_tabs, 1)
            dve.wait_ge(s_lT, 1)
            nc.vector.tensor_scalar(lb[:, :], pt[:, 0:NS], amx[:, 0:1], None, ALU.add).then_inc(s_tabs, 1)
            dve.wait_ge(s_tabs, 2)
            nc.vector.tensor_scalar(b1[:, :], lb[:, :], SLOPE - 1.0, None, ALU.mult).then_inc(s_tabs, 1)
            dve.wait_ge(s_tabs, 3)
            nc.vector.tensor_scalar(b2[:, :], lb[:, :], spread, 1.0 - SLOPE, ALU.subtract,
                                    ALU.mult).then_inc(s_setup, 1)
            dve.wait_ge(s_setup, 10)
            nc.vector.tensor_scalar(b2[:, :], b2[:, :], 0.0, None, ALU.min).then_inc(s_tabs, 1)
            nc.vector.tensor_scalar(X16[:, 0:JS, D], F[:, 0:JS], FSCALE, None, ALU.mult).then_inc(s_xrdy, 1)
            nc.vector.tensor_scalar(X[:, JS:JB, D], F[:, JS:JB], FSCALE * PSCALE, None, ALU.mult).then_inc(s_xrdy, 1)
            dve.wait_ge(s_xrdy, 1)
            nc.vector.scalar_tensor_tensor(out=X16[:, 0:JS, 2 * D + 2], in0=F[:, 0:JS], scalar=FSCALE,
                                           in1=X16[:, 0:JS, D], op0=ALU.mult, op1=ALU.subtract).then_inc(s_xrdy, 1)
            for j in range(JS):
                dve.wait_ge(s_xh, j + 1)
                nc.vector.scalar_tensor_tensor(out=X16[:, j, D + 2:2 * D + 2], in0=xs[:, j, :], scalar=Fx[:, j:j + 1],
                                               in1=X16[:, j, 0:D], op0=ALU.mult,
                                               op1=ALU.subtract).then_inc(s_xrdy, 1)
            dve.wait_ge(s_xh, JS)
            dve.wait_ge(s_x32, 1)
            dve.wait_ge(s_xrdy, JS + 3)
            dve.wait_ge(s_tabs, 4)
            general = dve.value_load(flag.bitcast(I32)[0:1, 0:1])

            def masked(n, b, k, use):
                s = strip[:, b, :]
                with dve.If(general == 0):
                    dve.wait_ge(s_adj[b], use * 16 * Q)
                    dve.wait_ge(s_wexp, n + 1)
                    nc.vector.scalar_tensor_tensor(out=s, in0=s, scalar=0.0, in1=w[:, k % 2, :], op0=ALU.is_gt,
                                                   op1=ALU.mult).then_inc(s_p, 1)
                with dve.Else():
                    dve.wait_ge(s_adj[b], use * 16 * Q)
                    step = [0]

                    def chain(m):
                        m.then_inc(s_gen, 1)
                        step[0] += 1
                        dve.wait_ge(s_gen, n * GEN + step[0])

                    chain(nc.vector.scalar_tensor_tensor(out=s, in0=s, scalar=0.0, in1=tab[:, :], op0=ALU.is_le,
                                                         op1=ALU.max))
                    chain(nc.vector.tensor_reduce(mnq, s, AX.X, ALU.min))
                    for q in range(Q):
                        chain(nc.vector.tensor_copy(c4[0:B, q:q + 1], mnq[q * B:(q + 1) * B, :]))
                    chain(nc.vector.tensor_reduce(m1[0:B, :], c4[0:B, :], AX.X, ALU.min))
                    for q in range(Q):
                        chain(nc.vector.tensor_copy(mn[q * B:(q + 1) * B, :], m1[0:B, :]))
                    lbn = lb[:, bass.ds(n, 1)]
                    chain(nc.vector.scalar_tensor_tensor(out=mnq, in0=mn, scalar=-BIG, in1=lbn, op0=ALU.mult,
                                                         op1=ALU.add))
                    chain(nc.vector.scalar_tensor_tensor(out=mn, in0=mnq, scalar=SLOPE, in1=mnq, op0=ALU.mult,
                                                         op1=ALU.max))
                    chain(nc.vector.tensor_scalar(nmax, mn, FLOOR, -1.0, ALU.max, ALU.mult))
                    chain(nc.vector.tensor_tensor(b1[:, bass.ds(n, 1)], lbn, nmax, ALU.add))
                    assert step[0] == GEN
                    nc.vector.scalar_tensor_tensor(out=b2[:, bass.ds(n, 1)], in0=lbn, scalar=SLOPE, in1=nmax,
                                                   op0=ALU.mult, op1=ALU.add).then_inc(s_z, 1)
                    dve.wait_ge(s_wexp, n + 1)
                    nc.vector.tensor_tensor(s, s, w[:, k % 2, :], ALU.max).then_inc(s_p, 1)

            def reciprocal(g, o):
                dve.wait_ge(s_psfree, g + 3)
                nc.vector.reciprocal(st(0, o), y[:, o, D:D + 1]).then_inc(s_rd, 1)

            def stats(g, o):
                dve.wait_ge(s_res, g + 1)
                nc.vector.bn_stats(small[:, 28 + 14 * o + 8:28 + 14 * o + 14], y[:, o, 0:D]).then_inc(s_bn, 1)

            def moments(g, o):
                dve.wait_ge(s_tabs, 2)
                dve.wait_ge(s_bn, g + 1)
                nc.vector.bn_aggr(small[:, 28 + 14 * o + 1:28 + 14 * o + 3],
                                  small[:, 28 + 14 * o + 8:28 + 14 * o + 14]).then_inc(s_mv, 1)

            def steps(it, last):
                for k in range(SI):
                    n, b, g, o = it * SI + k, k % NB, it * GI + k // SG, (k // SG) % 2
                    s0 = (k % SG) * B
                    if not (last and k == SI - 1):
                        use = (it * SI + k + 1) // NB + 1 if isinstance(it, int) else it * (SI // NB) + (k + 1) // NB + 1
                        masked(n + 1, (k + 1) % NB, k + 1, use)
                    dve.wait_ge(s_p, n + 1)
                    if k % SG == 0:
                        wait(dve, s_mm, g - 1)
                    dve.wait_ge(s_hi, n + 1)
                    nc.vector.scalar_tensor_tensor(out=pair16[:, k % 2, :, 1], in0=strip[:, b, 0:CS], scalar=PSCALE,
                                                   in1=pair16[:, k % 2, :, 0], op0=ALU.mult,
                                                   op1=ALU.subtract).then_inc(s_lo, 1)
                    nc.vector.transpose(T[:, o, JS:JB, s0:s0 + B],
                                        strip[:, b, CS:NQ].rearrange("p (j i) -> p j i", i=B)).then_inc(s_t32, 1)
                    if k % SG == 3 and (not isinstance(g, int) or g >= 2):
                        stats(g - 2, o)
                    dve.wait_ge(s_lo, n + 1)
                    nc.vector.transpose(T[:, o, 0:JS, s0:s0 + B],
                                        pair[:, k % 2, :].rearrange("p (j i) -> p j i", i=B)).then_inc(s_t16, 1)
                    if k % SG == 2 and (not isinstance(g, int) or g >= 2):
                        reciprocal(g - 2, o)
                    if k % SG == 3 and (not isinstance(g, int) or g >= 2):
                        moments(g - 2, o)

            masked(0, 0, 0, 1)
            steps(0, False)
            with dve.Fori(1, IT - 1) as it:
                steps(it, False)
            steps(IT - 1, True)
            for g in range(NG - 2, NG):
                reciprocal(g, g % 2)
                stats(g, g % 2)
                moments(g, g % 2)


_INS = ["x", "adj", "L0_gnn_context", "L0_gnn_W_common", "L0_gnn_w_left", "L0_gnn_b_left", "L0_gnn_w_right",
        "L0_gnn_b_right"]


def kernel(**inputs):
    import numpy as _np
    import concourse.bacc as _bacc
    from concourse import mybir as _mybir
    from concourse.bass_utils import run_bass_kernel_spmd as _run

    nc = _bacc.Bacc("TRN2", target_bir_lowering=False, num_devices=1)
    arrays, args = {}, []
    for name in _INS:
        a = _np.ascontiguousarray(inputs[name])
        if a.ndim == 0:
            a = a.reshape(1)
        arrays[f"in_{name}_dram"] = a
        args.append(nc.dram_tensor(f"in_{name}_dram", a.shape, _mybir.dt.from_np(a.dtype), kind="ExternalInput").ap())
    shape = inputs["x"].shape
    args.append(nc.dram_tensor("out_dram", shape, _mybir.dt.float32, kind="ExternalOutput").ap())
    build(nc, *args)
    r = _run(nc, [arrays], core_ids=[0])
    return r.results[0]["out_dram"]
```
